# Optimizing a Trainium2 kernel written in Bass

```python
import numpy as np
import jax
import jax.numpy as jnp

def _softmax(x, axis=-1):
    return jax.nn.softmax(x, axis=axis)

def _gelu(x):
    return jax.nn.gelu(x, approximate=True)

def _silu(x):
    return jax.nn.silu(x)

def _sigmoid(x):
    return jax.nn.sigmoid(x)

def _layernorm(x, axis=-1, eps=1e-05):
    m = jnp.mean(x, axis=axis, keepdims=True)
    v = jnp.var(x, axis=axis, keepdims=True)
    return (x - m) / jnp.sqrt(v + eps)

def _scatter_add(tgt, idx, src, axis=0):
    return tgt.at[idx].add(src)

def _segment_sum(src, seg, n):
    return jax.ops.segment_sum(src, seg, n)
kernel_name = 'mk_prb_d2_jaxref_r8_a2c755'

def setup_inputs(seed: int=0):
    np.random.seed(seed)
    _w = jnp.asarray

    def _L0_attn_setup():
        import jax, jax.numpy as jnp
        import numpy as np
        import math
        B, S, E, H = (2, 256, 128, 16)
        D = E // H
        key = jax.random.key(seed)
        ks = jax.random.split(key, 5)
        scale_p = 1.0 / math.sqrt(D)
        return {'x': jax.random.normal(ks[0], (B, S, E), dtype=jnp.float32), 'Wq': jax.random.normal(ks[1], (D, D), dtype=jnp.float32) * scale_p, 'Wk': jax.random.normal(ks[2], (D, D), dtype=jnp.float32) * scale_p, 'Wv': jax.random.normal(ks[3], (D, D), dtype=jnp.float32) * scale_p, 'W_out': jax.random.normal(ks[4], (E, E), dtype=jnp.float32) * (1.0 / math.sqrt(E)), 'b_out': jnp.zeros((E,), dtype=jnp.float32)}
    _L0_attn_in = _L0_attn_setup()

    def _L0_ffn_setup():
        import jax, jax.numpy as jnp
        import numpy as np
        B, S, D, H, L, E, K = (4, 128, 128, 16, 2, 8, 2)
        DFF = 4 * D

        def _ln(x, w, b):
            m = x.mean(-1, keepdims=True)
            v = x.var(-1, keepdims=True)
            return (x - m) / jnp.sqrt(v + 1e-05) * w + b

        def _attn(x, wq, wk, wv, wo, bq, bk, bv, bo):
            Bb, T, C = x.shape
            hd = C // H
            q = (x @ wq + bq).reshape(Bb, T, H, hd).transpose(0, 2, 1, 3)
            k = (x @ wk + bk).reshape(Bb, T, H, hd).transpose(0, 2, 1, 3)
            v = (x @ wv + bv).reshape(Bb, T, H, hd).transpose(0, 2, 1, 3)
            att = jnp.einsum('bhqd,bhkd->bhqk', q, k) * hd ** (-0.5)
            causal = jnp.tril(jnp.ones((T, T), bool))
            att = jnp.where(causal, att, -jnp.inf)
            att = jax.nn.softmax(att, axis=-1)
            y = jnp.einsum('bhqk,bhkd->bhqd', att, v).transpose(0, 2, 1, 3).reshape(Bb, T, C)
            return y @ wo + bo

        def _ffn(h, w1, b1, w2, b2):
            return jax.nn.gelu(h @ w1 + b1, approximate=False) @ w2 + b2

        def _combine_weights(logits):
            vals, idx = jax.lax.top_k(logits, K)
            w = jax.nn.softmax(vals, axis=-1)
            onehot = (idx[..., None] == jnp.arange(E)).astype(w.dtype)
            return jnp.sum(w[..., None] * onehot, axis=-2)

        def _token_moe(h, gw, gb, w1, b1, w2, b2):
            cw = _combine_weights(h @ gw + gb)
            out = jnp.zeros_like(h)
            for e in range(E):
                out = out + _ffn(h, w1[e], b1[e], w2[e], b2[e]) * cw[..., e:e + 1]
            return out

        def _seq_moe(h, gw, gb, w1, b1, w2, b2):
            cw = _combine_weights(h.mean(axis=1) @ gw + gb)
            out = jnp.zeros_like(h)
            for e in range(E):
                out = out + _ffn(h, w1[e], b1[e], w2[e], b2[e]) * cw[:, e, None, None]
            return out
        key = jax.random.key(seed)
        ks = jax.random.split(key, 9)
        n = lambda k, shp: jax.random.normal(k, shp, dtype=jnp.float32) * 0.02
        return {'x': jax.random.normal(ks[0], (B, S, D), dtype=jnp.float32), 'ln1_w': jnp.ones((L, D), jnp.float32), 'ln1_b': jnp.zeros((L, D), jnp.float32), 'ln2_w': jnp.ones((L, D), jnp.float32), 'ln2_b': jnp.zeros((L, D), jnp.float32), 'wq': n(ks[1], (L, D, D)), 'wk': n(ks[2], (L, D, D)), 'wv': n(ks[3], (L, D, D)), 'wo': n(ks[4], (L, D, D)), 'bq': jnp.zeros((L, D), jnp.float32), 'bk': jnp.zeros((L, D), jnp.float32), 'bv': jnp.zeros((L, D), jnp.float32), 'bo': jnp.zeros((L, D), jnp.float32), 'gate_w': n(ks[5], (L, D, E)), 'gate_b': jnp.zeros((L, E), jnp.float32), 'e_w1': n(ks[6], (L, E, D, DFF)), 'e_b1': jnp.zeros((L, E, DFF), jnp.float32), 'e_w2': n(ks[7], (L, E, DFF, D)), 'e_b2': jnp.zeros((L, E, D), jnp.float32)}
    _L0_ffn_in = _L0_ffn_setup()

    def _L1_attn_setup():
        import jax, jax.numpy as jnp
        import numpy as np
        import math
        D_MODEL = 128
        NUM_HEADS = 16
        HEAD = D_MODEL // NUM_HEADS
        EPS = 1e-05

        def _layernorm(x, w, b):
            mean = jnp.mean(x, axis=-1, keepdims=True)
            var = jnp.var(x, axis=-1, keepdims=True)
            return (x - mean) * w / jnp.sqrt(var + EPS) + b
        key = jax.random.key(seed)
        ks = jax.random.split(key, 5)
        x = jax.random.normal(ks[0], (2, 256, D_MODEL), dtype=jnp.float32)
        wq = jax.random.uniform(ks[1], (NUM_HEADS, D_MODEL, HEAD), dtype=jnp.float32) * 0.02
        wk = jax.random.uniform(ks[2], (NUM_HEADS, D_MODEL, HEAD), dtype=jnp.float32) * 0.02
        wv = jax.random.uniform(ks[3], (NUM_HEADS, D_MODEL, HEAD), dtype=jnp.float32) * 0.02
        wo = jax.random.uniform(ks[4], (D_MODEL, D_MODEL), dtype=jnp.float32) * 0.02
        ln_w = jnp.ones((D_MODEL,), dtype=jnp.float32)
        ln_b = jnp.zeros((D_MODEL,), dtype=jnp.float32)
        return {'x': x, 'ln_w': ln_w, 'ln_b': ln_b, 'wq': wq, 'wk': wk, 'wv': wv, 'wo': wo}
    _L1_attn_in = _L1_attn_setup()

    def _L1_ffn_setup():
        import jax, jax.numpy as jnp
        import numpy as np
        TOP_K = 2
        EPS = 1e-09
        key = jax.random.key(seed)
        ks = jax.random.split(key, 6)
        B, T, D, H, E = (4, 256, 128, 256, 8)
        x = jax.random.normal(ks[0], (B, T, D), dtype=jnp.float32)
        Wg = jax.random.normal(ks[1], (E, D), dtype=jnp.float32) * 0.02
        W1 = jax.random.normal(ks[2], (E, 2 * H, D), dtype=jnp.float32) * 0.02
        b1 = jax.random.normal(ks[3], (E, 2 * H), dtype=jnp.float32) * 0.02
        Wo = jax.random.normal(ks[4], (D, H), dtype=jnp.float32) * 0.02
        bo = jax.random.normal(ks[5], (D,), dtype=jnp.float32) * 0.02
        return {'x': x, 'Wg': Wg, 'W1': W1, 'b1': b1, 'Wo': Wo, 'bo': bo}
    _L1_ffn_in = _L1_ffn_setup()
    _d = {'L0_attn_x': _L0_attn_in['x'], 'L0_attn_Wq': _L0_attn_in['Wq'], 'L0_attn_Wk': _L0_attn_in['Wk'], 'L0_attn_Wv': _L0_attn_in['Wv'], 'L0_attn_W_out': _L0_attn_in['W_out'], 'L0_attn_b_out': _L0_attn_in['b_out'], 'L0_ffn_ln1_w': _L0_ffn_in['ln1_w'], 'L0_ffn_ln1_b': _L0_ffn_in['ln1_b'], 'L0_ffn_ln2_w': _L0_ffn_in['ln2_w'], 'L0_ffn_ln2_b': _L0_ffn_in['ln2_b'], 'L0_ffn_wq': _L0_ffn_in['wq'], 'L0_ffn_wk': _L0_ffn_in['wk'], 'L0_ffn_wv': _L0_ffn_in['wv'], 'L0_ffn_wo': _L0_ffn_in['wo'], 'L0_ffn_bq': _L0_ffn_in['bq'], 'L0_ffn_bk': _L0_ffn_in['bk'], 'L0_ffn_bv': _L0_ffn_in['bv'], 'L0_ffn_bo': _L0_ffn_in['bo'], 'L0_ffn_gate_w': _L0_ffn_in['gate_w'], 'L0_ffn_gate_b': _L0_ffn_in['gate_b'], 'L0_ffn_e_w1': _L0_ffn_in['e_w1'], 'L0_ffn_e_b1': _L0_ffn_in['e_b1'], 'L0_ffn_e_w2': _L0_ffn_in['e_w2'], 'L0_ffn_e_b2': _L0_ffn_in['e_b2'], 'L1_attn_ln_w': _L1_attn_in['ln_w'], 'L1_attn_ln_b': _L1_attn_in['ln_b'], 'L1_attn_wq': _L1_attn_in['wq'], 'L1_attn_wk': _L1_attn_in['wk'], 'L1_attn_wv': _L1_attn_in['wv'], 'L1_attn_wo': _L1_attn_in['wo'], 'L1_ffn_Wg': _L1_ffn_in['Wg'], 'L1_ffn_W1': _L1_ffn_in['W1'], 'L1_ffn_b1': _L1_ffn_in['b1'], 'L1_ffn_Wo': _L1_ffn_in['Wo'], 'L1_ffn_bo': _L1_ffn_in['bo']}
    _x0 = _d['L0_attn_x']
    _d['L0_attn_x'] = jax.random.normal(jax.random.fold_in(jax.random.key(seed), 1), (4, 512, 128), dtype=_x0.dtype)
    del _x0
    return _d

def reference(L0_attn_x, L0_attn_Wq, L0_attn_Wk, L0_attn_Wv, L0_attn_W_out, L0_attn_b_out, L0_ffn_ln1_w, L0_ffn_ln1_b, L0_ffn_ln2_w, L0_ffn_ln2_b, L0_ffn_wq, L0_ffn_wk, L0_ffn_wv, L0_ffn_wo, L0_ffn_bq, L0_ffn_bk, L0_ffn_bv, L0_ffn_bo, L0_ffn_gate_w, L0_ffn_gate_b, L0_ffn_e_w1, L0_ffn_e_b1, L0_ffn_e_w2, L0_ffn_e_b2, L1_attn_ln_w, L1_attn_ln_b, L1_attn_wq, L1_attn_wk, L1_attn_wv, L1_attn_wo, L1_ffn_Wg, L1_ffn_W1, L1_ffn_b1, L1_ffn_Wo, L1_ffn_bo):

    def _L0_attn_ref(x, Wq, Wk, Wv, W_out, b_out):
        import jax, jax.numpy as jnp
        import numpy as np
        import math
        B, S, E, H = (2, 256, 128, 16)
        D = E // H
        b, s, e = x.shape
        xh = x.reshape(b, s, H, D)
        q = jnp.einsum('bshd,ed->bshe', xh, Wq)
        k = jnp.einsum('bshd,ed->bshe', xh, Wk)
        v = jnp.einsum('bshd,ed->bshe', xh, Wv)
        energy = jnp.einsum('bqhd,bkhd->bhqk', q, k) / jnp.sqrt(jnp.float32(e))
        attn = jax.nn.softmax(energy, axis=-1)
        out = jnp.einsum('bhqk,bkhd->bqhd', attn, v).reshape(b, s, e)
        return out @ W_out.T + b_out

    def _L0_ffn_ref(x, ln1_w, ln1_b, ln2_w, ln2_b, wq, wk, wv, wo, bq, bk, bv, bo, gate_w, gate_b, e_w1, e_b1, e_w2, e_b2):
        import jax, jax.numpy as jnp
        import numpy as np
        B, S, D, H, L, E, K = (4, 128, 128, 16, 2, 8, 2)
        DFF = 4 * D

        def _ln(x, w, b):
            m = x.mean(-1, keepdims=True)
            v = x.var(-1, keepdims=True)
            return (x - m) / jnp.sqrt(v + 1e-05) * w + b

        def _attn(x, wq, wk, wv, wo, bq, bk, bv, bo):
            Bb, T, C = x.shape
            hd = C // H
            q = (x @ wq + bq).reshape(Bb, T, H, hd).transpose(0, 2, 1, 3)
            k = (x @ wk + bk).reshape(Bb, T, H, hd).transpose(0, 2, 1, 3)
            v = (x @ wv + bv).reshape(Bb, T, H, hd).transpose(0, 2, 1, 3)
            att = jnp.einsum('bhqd,bhkd->bhqk', q, k) * hd ** (-0.5)
            causal = jnp.tril(jnp.ones((T, T), bool))
            att = jnp.where(causal, att, -jnp.inf)
            att = jax.nn.softmax(att, axis=-1)
            y = jnp.einsum('bhqk,bhkd->bhqd', att, v).transpose(0, 2, 1, 3).reshape(Bb, T, C)
            return y @ wo + bo

        def _ffn(h, w1, b1, w2, b2):
            return jax.nn.gelu(h @ w1 + b1, approximate=False) @ w2 + b2

        def _combine_weights(logits):
            vals, idx = jax.lax.top_k(logits, K)
            w = jax.nn.softmax(vals, axis=-1)
            onehot = (idx[..., None] == jnp.arange(E)).astype(w.dtype)
            return jnp.sum(w[..., None] * onehot, axis=-2)

        def _token_moe(h, gw, gb, w1, b1, w2, b2):
            cw = _combine_weights(h @ gw + gb)
            out = jnp.zeros_like(h)
            for e in range(E):
                out = out + _ffn(h, w1[e], b1[e], w2[e], b2[e]) * cw[..., e:e + 1]
            return out

        def _seq_moe(h, gw, gb, w1, b1, w2, b2):
            cw = _combine_weights(h.mean(axis=1) @ gw + gb)
            out = jnp.zeros_like(h)
            for e in range(E):
                out = out + _ffn(h, w1[e], b1[e], w2[e], b2[e]) * cw[:, e, None, None]
            return out
        for l in range(L):
            x = x + _attn(_ln(x, ln1_w[l], ln1_b[l]), wq[l], wk[l], wv[l], wo[l], bq[l], bk[l], bv[l], bo[l])
            h = _ln(x, ln2_w[l], ln2_b[l])
            moe = _token_moe if l % 2 == 0 else _seq_moe
            x = x + moe(h, gate_w[l], gate_b[l], e_w1[l], e_b1[l], e_w2[l], e_b2[l])
        return x

    def _L1_attn_ref(x, ln_w, ln_b, wq, wk, wv, wo):
        import jax, jax.numpy as jnp
        import numpy as np
        import math
        D_MODEL = 128
        NUM_HEADS = 16
        HEAD = D_MODEL // NUM_HEADS
        EPS = 1e-05

        def _layernorm(x, w, b):
            mean = jnp.mean(x, axis=-1, keepdims=True)
            var = jnp.var(x, axis=-1, keepdims=True)
            return (x - mean) * w / jnp.sqrt(var + EPS) + b
        y = _layernorm(x, ln_w, ln_b)
        seq_len = y.shape[-2]
        q = jnp.einsum('bsd,hde->bhse', y, wq)
        k = jnp.einsum('bsd,hde->bhse', y, wk)
        v = jnp.einsum('bsd,hde->bhse', y, wv)
        scores = jnp.einsum('bhse,bhte->bhst', q, k) / math.sqrt(HEAD)
        causal = jnp.triu(jnp.full((seq_len, seq_len), -jnp.inf, dtype=scores.dtype), k=1)
        scores = scores + causal
        weights = jax.nn.softmax(scores, axis=-1)
        attn = jnp.einsum('bhst,bhte->bshe', weights, v)
        attn = attn.reshape(*attn.shape[:-2], -1)
        out = attn @ wo
        return out + x

    def _L1_ffn_ref(x, Wg, W1, b1, Wo, bo):
        import jax, jax.numpy as jnp
        import numpy as np
        TOP_K = 2
        EPS = 1e-09
        E = Wg.shape[0]
        gate_logits = jnp.einsum('btd,ed->bte', x, Wg)
        gate_scores = jax.nn.softmax(gate_logits, axis=-1)
        topk_val, topk_idx = jax.lax.top_k(gate_scores, TOP_K)
        topk_val = topk_val / (topk_val.sum(axis=-1, keepdims=True) + EPS)
        comb = (jax.nn.one_hot(topk_idx, E, dtype=x.dtype) * topk_val[..., None]).sum(axis=-2)
        out = jnp.zeros_like(x)
        for e in range(E):
            h = jnp.einsum('btd,hd->bth', x, W1[e]) + b1[e]
            a, b = jnp.split(h, 2, axis=-1)
            g = a * jax.nn.sigmoid(b)
            eo = jnp.einsum('bth,dh->btd', g, Wo) + bo
            out = out + eo * comb[..., e:e + 1]
        return out
    x = L0_attn_x
    xn = _layernorm(x, axis=-1)
    x = x + _L0_attn_ref(xn, L0_attn_Wq, L0_attn_Wk, L0_attn_Wv, L0_attn_W_out, L0_attn_b_out) + _L0_ffn_ref(xn, L0_ffn_ln1_w, L0_ffn_ln1_b, L0_ffn_ln2_w, L0_ffn_ln2_b, L0_ffn_wq, L0_ffn_wk, L0_ffn_wv, L0_ffn_wo, L0_ffn_bq, L0_ffn_bk, L0_ffn_bv, L0_ffn_bo, L0_ffn_gate_w, L0_ffn_gate_b, L0_ffn_e_w1, L0_ffn_e_b1, L0_ffn_e_w2, L0_ffn_e_b2)
    xn = _layernorm(x, axis=-1)
    x = x + _L1_attn_ref(xn, L1_attn_ln_w, L1_attn_ln_b, L1_attn_wq, L1_attn_wk, L1_attn_wv, L1_attn_wo) + _L1_ffn_ref(xn, L1_ffn_Wg, L1_ffn_W1, L1_ffn_b1, L1_ffn_Wo, L1_ffn_bo)
    return x

_drawn_inputs = setup_inputs


def setup_inputs(seed=0):
    import zlib

    import numpy as np

    out = dict(_drawn_inputs(seed))
    spreads = {'L0_attn_b_out': (0.0, 1.26),
     'L0_ffn_ln1_w': (1.0, 0.6),
     'L0_ffn_ln1_b': (0.0, 0.8),
     'L0_ffn_ln2_w': (1.0, 0.6),
     'L0_ffn_ln2_b': (0.0, 2.0),
     'L0_ffn_bq': (0.0, 0.8),
     'L0_ffn_bk': (0.0, 2.0),
     'L0_ffn_bv': (0.0, 1.341),
     'L0_ffn_bo': (0.0, 0.666),
     'L0_ffn_gate_b': (0.0, 1.024),
     'L0_ffn_e_b1': (0.0, 2.0),
     'L0_ffn_e_b2': (0.0, 1.112),
     'L1_attn_ln_w': (1.0, 0.6),
     'L1_attn_ln_b': (0.0, 0.8)}
    factors = {'L0_ffn_wq': 8.0,
     'L0_ffn_wk': 8.0,
     'L0_ffn_wv': 8.0,
     'L0_ffn_wo': 3.095,
     'L1_attn_wq': 27.213,
     'L1_attn_wk': 33.275,
     'L1_attn_wv': 8.0,
     'L1_attn_wo': 8.0,
     'L1_ffn_Wg': 7.477,
     'L1_ffn_W1': 6.564,
     'L1_ffn_b1': 49.576,
     'L1_ffn_Wo': 6.503,
     'L1_ffn_bo': 46.131,
     'L0_attn_Wq': 3.821,
     'L0_attn_Wk': 3.334,
     'L0_attn_Wv': 4.163,
     'L0_attn_W_out': 3.99,
     'L0_ffn_gate_w': 3.735,
     'L0_ffn_e_w1': 4.748,
     'L0_ffn_e_w2': 3.793}
    for name, (base, spread) in spreads.items():
        noise = np.random.default_rng([zlib.crc32(name.encode()), seed]).standard_normal(out[name].shape)
        drawn = base * np.exp(spread * noise) if base else spread * noise
        out[name] = jnp.asarray(drawn.astype(out[name].dtype))
    for name, factor in factors.items():
        out[name] = (out[name] * factor).astype(out[name].dtype)
    return out
```

```python
import concourse.bass as bass
from concourse import mybir
from contextlib import ExitStack

F32 = mybir.dt.float32
F32R = mybir.dt.float32r
BF16 = mybir.dt.bfloat16
U32 = mybir.dt.uint32
ALU = mybir.AluOpType
ACT = mybir.ActivationFunctionType
AX = mybir.AxisListType

P = 128
BATCH = 4
S = 512
D = 128
NT = S // P
H = 16
HD = D // H
G = 4
HG = H // G
E = 8
DFF = 512
NC = DFF // P
GLU = 256
NEG = -1e30
EPS = 1e-5
BIG = 2048

A0, B1, B2, C3 = range(4)
CAUSAL = (False, True, True, True)
SCALE = (float(D) ** -0.5, float(HD) ** -0.5, float(HD) ** -0.5, float(HD) ** -0.5)
CHAIN = 55

LN_IN, LN_A1, LN_M1, LN_A2, LN_M2, LN_MID, LN_C = range(7)
LN_OF_ATT = {A0: LN_IN, B1: LN_A1, B2: LN_A2, C3: LN_C}
COL_LN = {LN_A1: 0, LN_M1: 2, LN_A2: 4, LN_M2: 6, LN_C: 8}
COL_QB = {B1: 10, B2: 12}
COL_EB1 = 14
N_COLS = COL_EB1 + E * NC
TOKEN, SEQ, GATED = range(3)


def max_pieces(a):
    out = []
    for qt in range(NT):
        width = (qt + 1) * P if CAUSAL[a] else S
        n = S // width
        out += [(qt, range(j, min(j + n, HG))) for j in range(0, HG, n)]
    return out


def prob_pieces(a):
    out = []
    for kt in range(NT):
        width = S - kt * P if CAUSAL[a] else S
        n = min(HG, 2 * (S // width))
        out += [(kt, range(j, j + n)) for j in range(0, HG, n)]
    return out


def attention_steps(a):
    maxima, wait_nm = [], []
    for g in range(G):
        pieces = [("max", g, i) for i in range(len(max_pieces(a)))]
        maxima.append(pieces)
    stream = [m for g in range(G) for m in maxima[g]]
    per_group = len(maxima[0])
    probs = prob_pieces(a)
    steps = list(stream[:per_group]) + [("negmax", 0)]
    sent, due = per_group, []
    out_due = None
    for g in range(G):
        for i, (kt, heads) in enumerate(probs):
            steps.append(("prob", g, i))
            if wait_nm:
                steps.append(wait_nm.pop())
            goal = per_group * (g + 1) + min(per_group, -(-per_group * (i + 1) * 8 // (len(probs) * 6)))
            while sent < min(goal, len(stream)):
                steps.append(stream[sent])
                sent += 1
                if sent % per_group == 0:
                    wait_nm.append(("negmax", sent // per_group - 1))
            if i == 1 and out_due is not None:
                steps.append(("unstack", out_due))
                out_due = None
            last_of_tile = i + 1 == len(probs) or probs[i + 1][0] != kt
            if last_of_tile:
                if due:
                    steps.append(due.pop())
                due.append(("value", g, kt))
        if wait_nm:
            steps.append(wait_nm.pop())
        steps.append(due.pop())
        out_due = g
    steps.append(("unstack", G - 1))
    return steps


class Signal:

    def __init__(self, sem, keys, by=1):
        self.sem, self.keys, self.by, self.next = sem, list(keys), by, 0
        self.at_key = {k: n for n, k in enumerate(self.keys)}
        assert len(self.at_key) == len(self.keys)

    def at(self, turn, key):
        return self.sem, turn * (len(self.keys) * self.by) + (self.at_key[key] + 1) * self.by

    def by_key(self, key):
        assert self.keys[self.next % len(self.keys)] == key, (self.keys[self.next % len(self.keys)], key)
        self.next += 1
        return self.sem, self.by


class Bank:

    def __init__(self, sem, name, uses, turn_free):
        self.fill = Signal(sem(f"{name}_filled"), [k for k, _ in uses])
        self.empty = {who: Signal(sem(f"{name}_emptied_{who}"), [k for k, w in uses if w == who])
                      for who in ("act", "dve")}
        self.who, self.turn_free = dict(uses), turn_free

    def free(self, turn, key):
        n = self.fill.at_key[key]
        return self.emptied(turn, self.fill.keys[n - 1]) if n else (self.turn_free, turn + 1)

    def filled(self, turn, key):
        return self.fill.at(turn, key)

    def emptied(self, turn, key):
        return self.empty[self.who[key]].at(turn, key)

    def fills(self, key):
        return self.fill.by_key(key)

    def empties(self, key):
        return self.empty[self.who[key]].by_key(key)


def build(nc, x, w_att, cols, bv_rows, out_rows, gate_w, gate_rows, w1_token, w2_token, eb2, w1_seq, b1_seq,
          w2_seq, w1_glu, b1_glu, wo_glu, bo_glu, out):
    ctx = ExitStack()
    with ctx:
        def sb(name, shape, dt=F32):
            return ctx.enter_context(nc.sbuf_tensor(name, shape, dt))

        def sem(name):
            return ctx.enter_context(nc.semaphore(name))

        ident = sb("ident", [P, P])
        ident_b = sb("ident_b", [P, P], BF16)
        causal_b = sb("causal_b", [P, P], BF16)
        causal_kq = sb("causal_kq", [P, P], BF16)
        ones_b = sb("ones_b", [3, P], BF16)
        iota8 = sb("iota8", [P, E])
        minus_half = sb("minus_half", [P, NT])
        watt = sb("watt", [P, 4, 4, D])
        col = sb("col", [P, N_COLS])
        bv_bc = sb("bv_bc", [P, 2, D])
        out_bc = sb("out_bc", [P, 3, D])
        gate_bc = sb("gate_bc", [P, 2, E])
        bo_bc = sb("bo_bc", [P, D])
        gw = sb("gw", [P, 3, E])
        eb2_sb = sb("eb2_sb", [E, 2, D])
        w1_hi = sb("w1_hi", [P, E, DFF], F32R)
        w1_lo = sb("w1_lo", [P, E, DFF], F32R)
        w2_sb = sb("w2_sb", [P, E, NC, D])
        wg_hi = sb("wg_hi", [P, E, 2 * GLU], F32R)
        wg_lo = sb("wg_lo", [P, E, 2 * GLU], F32R)
        b1g3 = sb("b1g3", [3, E * 2 * GLU], BF16)
        wog = sb("wog", [P, 2, D])

        x_in = sb("x_in", [P, NT, D])
        xn = sb("xn", [P, NT, D])
        att_a = x_in
        res = sb("res", [P, NT, D])
        z = sb("z", [P, NT, D])
        y_out = x_in
        hT = sb("hT", [P, S])
        h_hi = sb("h_hi", [P, S], F32R)
        h_lo = sb("h_lo", [P, S], F32R)
        parts = sb("parts", [P, 4, S], F32R)
        q_hi, q_lo, k_hi, k_lo = (parts[:, n, :] for n in range(4))
        ws_hi, ws_lo = parts[:, 0:2, :], parts[:, 2:4, :]
        q_stack = sb("q_stack", [P, 2, S], F32R)
        k_stack = sb("k_stack", [P, G, S], F32R)
        q_head = sb("q_head", [P, H, S], F32R)
        v_ones = sb("v_ones", [P, NT, H, 32])
        probs = sb("probs", [P, 3, BIG])
        mx = sb("mx", [P, 2, HG * NT])
        negmax = sb("negmax", [HG * NT, 2, P], F32R)
        o_sb = sb("o_sb", [P, 2, S])
        rden = sb("rden", [P, NT, HG])
        att = z
        attT = o_sb[:, 0, :]
        stats = sb("stats", [P, NT, 6])
        mv = sb("mv", [P, NT, 2])
        var_eps = sb("var_eps", [P, NT])
        rstd = sb("rstd", [P, NT])
        h_mean = sb("h_mean", [P, 1])
        h_mean_bc = o_sb[:, 0, 0:P]
        lg = sb("lg", [P, NT, E])
        v8 = sb("v8", [P, NT, 8])
        i8 = sb("i8", [P, NT, 8], U32)
        i_f = sb("i_f", [P, NT, 2])
        ex_in = sb("ex_in", [P, NT, 9])
        ex = sb("ex", [P, NT, 9])
        den = sb("den", [P, NT])
        w_first = sb("w_first", [P, NT])
        w_second = sb("w_second", [P, NT])
        w_sum = sb("w_sum", [P, NT])
        cw1 = sb("cw1", [P, NT, E])
        cw2 = sb("cw2", [P, NT, E])
        cw = sb("cw", [P, NT, E])
        cwT = o_sb[0:E, 1, :]
        b1_raw = sb("b1_raw", [P, 2, NC])

        stage = probs[:, 0:2, :].rearrange("p a (e n) -> p (a e) n", n=DFF)
        B1_COLS = E * 2 * GLU // P
        b1_rest = o_sb[:, 0, 0:3 * B1_COLS].rearrange("p (a n) -> p a n", a=3)
        b1_parts = sb("b1_parts", [P, 3, B1_COLS], BF16)
        gluT = probs[:, 0, 0:2 * S].rearrange("p (c n) -> p c n", c=2)
        glu_acc = probs[:, 0, 2 * S:BIG].rearrange("p (t n) -> p t n", t=NT)
        glu_sig = probs[:, 1, 0:4 * GLU].rearrange("p (a k n) -> p a k n", a=2, k=2)
        glu_u = probs[:, 1, 4 * GLU:BIG].rearrange("p (a n) -> p a n", a=4)

        ps_s = ctx.enter_context(nc.psum_tensor("ps_s", [P, 2, S], F32))
        ps_t = ctx.enter_context(nc.psum_tensor("ps_t", [P, 2, 2 * S], F32))
        ps_o = ctx.enter_context(nc.psum_tensor("ps_o", [P, S], F32))
        ps_m = ctx.enter_context(nc.psum_tensor("ps_m", [P, S], F32))

        STEPS = [attention_steps(a) for a in range(4)]

        s_uses, t_uses, o_uses, m_uses, slot_uses = ([], []), ([], []), [], [], []
        s_count = [0]
        s_bank, t_slot, p_slot = {}, {}, {}

        def use_s(key, who):
            s_bank[key] = s_count[0] % 2
            s_uses[s_count[0] % 2].append((key, who))
            s_count[0] += 1

        t_count = [0]

        def use_t(key, who):
            t_slot[key] = t_count[0] % 2
            t_uses[t_count[0] % 2].append((key, who))
            t_count[0] += 1

        def use_slot(key):
            p_slot[key] = len(slot_uses) % 3
            slot_uses.append(key)

        def plan_ln(n):
            m_uses.append((("ln", n), "dve"))

        def plan_attention(a):
            use_s(("q", a), "dve")
            use_s(("k", a), "dve")
            m_uses.append((("v", a), "dve"))
            for step in STEPS[a]:
                if step[0] == "max":
                    use_s((a, *step), "dve")
                elif step[0] == "negmax":
                    m_uses.append(((a, *step), "act"))
                elif step[0] == "prob":
                    use_t((a, *step), "act")
                elif step[0] == "unstack":
                    o_uses.append(((a, step[1]), "act"))
                    m_uses.append(((a, *step), "dve"))
            for g in range(G):
                for kt in range(NT):
                    use_slot((a, g, kt))
            m_uses.append((("attT", a), "act"))
            m_uses.append((("y", a), "dve"))

        def plan_gelu_moe(m):
            m_uses.append((("logits", m), "dve"))
            for e in range(E if m == TOKEN else 2):
                for half in range(2):
                    use_t(("up", m, e, half), "act")
                use_slot((m, e))
            m_uses.append((("cwT", m), "act"))
            m_uses.append((("b2", m), "dve"))
            for e in range(E if m == TOKEN else 2):
                use_s(("down", m, e), "dve")

        def plan_glu_moe():
            m_uses.append((("logits", GATED), "dve"))
            for t in range(NT):
                for pair in range(E // 2):
                    use_t(("glu", t, pair), "dve")
            use_t(("gluT",), "act")
            m_uses.append((("glu_y",), "dve"))

        plan_ln(LN_IN)
        plan_attention(A0)
        plan_ln(LN_A1)
        plan_attention(B1)
        plan_ln(LN_M1)
        plan_gelu_moe(TOKEN)
        plan_ln(LN_A2)
        plan_attention(B2)
        plan_ln(LN_M2)
        plan_gelu_moe(SEQ)
        plan_ln(LN_MID)
        plan_glu_moe()
        plan_ln(LN_C)
        plan_attention(C3)

        spare = ({0, 1, 2} - {p_slot[(SEQ, 0)], p_slot[(SEQ, 1)]}).pop()
        w1_raw = probs[:, spare, 0:2 * DFF].rearrange("p (k n) -> p k n", k=2)
        w2_raw = probs[:, spare, 2 * DFF:BIG].rearrange("p (k c d) -> p k c d", k=2, c=NC)

        turn_free = sem("turn_free")
        bank_s = [Bank(sem, f"s{n}", s_uses[n], turn_free) for n in range(2)]
        slot_t = [Bank(sem, f"t{n}", t_uses[n], turn_free) for n in range(2)]
        bank_o = Bank(sem, "o", o_uses, turn_free)
        bank_m = Bank(sem, "m", m_uses, turn_free)

        def S_of(key):
            return bank_s[s_bank[key]], ps_s[:, s_bank[key], :]

        def T_of(key):
            return slot_t[t_slot[key]], ps_t[:, t_slot[key], :]

        def probs_of(key):
            return probs[:, p_slot[key], :]

        ATTS = range(4)
        GROUPS = [(a, g) for a in ATTS for g in range(G)]
        NEGMAX = [(a, step[1]) for a in ATTS for step in STEPS[a] if step[0] == "negmax"]
        x_loaded = Signal(sem("x_loaded"), ["x"], 16)
        q_stack_loaded, k_stack_loaded = (
            [Signal(sem(f"{w}_stack{g}_loaded"), [(a, n) for a in ATTS for n in range(3)], 16) for g in range(G)]
            for w in "qk")
        head_loaded = [Signal(sem(f"head{g}_loaded"), [(a, j) for a in ATTS for j in range(HG)], 16)
                       for g in range(G)]
        negmax_loaded = Signal(sem("negmax_loaded"), NEGMAX, 16)
        seq_w_loaded = Signal(sem("seq_w_loaded"), range(6), 16)
        stored = Signal(sem("stored"), ["out"], 16)
        z_ready = Signal(sem("z_ready"), range(7))
        var_ready = Signal(sem("var_ready"), range(7))
        rstd_ready = Signal(sem("rstd_ready"), range(7))
        HALVES = [LN_M1, LN_M2, LN_MID]
        hi_ready = Signal(sem("hi_ready"), HALVES)
        lo_ready = Signal(sem("lo_ready"), HALVES)
        qk_hi_ready = Signal(sem("qk_hi_ready"), [(a, w) for a in ATTS for w in "qk"])
        slot_read = Signal(sem("slot_read"), [k for k in slot_uses if len(k) == 3 and k[2] < NT - 1])
        h_mean_ready = Signal(sem("h_mean_ready"), [SEQ])
        gate_in_ready = Signal(sem("gate_in_ready"), (TOKEN, SEQ, GATED))
        gate_exp_ready = Signal(sem("gate_exp_ready"), (TOKEN, SEQ, GATED))
        index_ready = Signal(sem("index_ready"), (TOKEN, SEQ, GATED))
        cw_ready = Signal(sem("cw_ready"), (TOKEN, SEQ, GATED))
        seq_hi_ready = Signal(sem("seq_hi_ready"), [SEQ])
        seq_lo_ready = Signal(sem("seq_lo_ready"), [SEQ])
        PAIRS = [(t, pair) for t in range(NT) for pair in range(E // 2)]
        sig_ready = Signal(sem("sig_ready"), PAIRS)
        u_added = Signal(sem("u_added"), [(t, e) for t in range(NT) for e in range(1, E)])
        y_ready = Signal(sem("y_ready"), ["y"])
        chained = sem("chained")

        def slot_free(turn, key):
            n = slot_uses.index(key)
            if n < 3:
                return turn_free, turn + 1
            before = slot_uses[n - 3]
            if len(before) == 2:
                down = ("down", *before)
                return S_of(down)[0].filled(turn, down)
            if before[2] == NT - 1:
                return bank_o.filled(turn, before[:2])
            return slot_read.at(turn, before)

        dve_passed, sp_passed = sem("dve_passed"), sem("sp_passed")

        loaded = sem("loaded")
        stage_loaded = [sem("stage0_loaded"), sem("stage1_loaded")]
        stage_hi, stage_lo = sem("stage_hi"), sem("stage_lo")
        b1_loaded, b1_split, b1_placed = sem("b1_loaded"), sem("b1_split"), sem("b1_placed")
        b1_subtracted = sem("b1_subtracted")
        pool_setup = sem("pool_setup")

        block = ctx.enter_context(nc.Block())

        @block.sync
        def _(sp):
            loads = [(watt[:, :, :, :], w_att), (col[:, :], cols), (gw[:, :, :], gate_w), (eb2_sb[:, :, :], eb2),
                     (bv_bc[:, :, :], bv_rows.partition_broadcast(P)), (out_bc[:, :, :], out_rows.partition_broadcast(P)),
                     (gate_bc[:, :, :], gate_rows.partition_broadcast(P)), (bo_bc[:, :], bo_glu.partition_broadcast(P)),
                     (wog[:, :, :], wo_glu), (w2_sb[:, 0:4, :, :], w2_token[:, 0:4]), (w2_sb[:, 4:8, :, :], w2_token[:, 4:8])]
            for dst, src in loads:
                sp.dma_start(dst, src).then_inc(loaded, 16)
            for n, (w, e0) in enumerate([(w1_token, 0), (w1_token, 4), (w1_glu, 0), (w1_glu, 4)]):
                if n >= 2:
                    sp.wait_ge(stage_lo, n - 1)
                sp.dma_start(stage[:, 4 * (n % 2):4 * (n % 2) + 4, :], w[:, e0:e0 + 4, :]).then_inc(stage_loaded[n % 2], 16)
            sp.dma_start(b1_rest[:, 0, :], b1_glu).then_inc(b1_loaded, 16)
            sp.wait_ge(b1_split, 3)
            for part in range(3):
                sp.dma_start(b1g3[part:part + 1, :], b1_parts[:, part, :]).then_inc(b1_placed, 16)

            def alone():
                sp.sem_inc(sp_passed, 1)

            def stack_loads(b, a, g):
                if a:
                    last = (a - 1, "prob", g, len(prob_pieces(a - 1)) - 1)
                    sp.wait_ge(*T_of(last)[0].filled(b, last))
                    alone()
                if g >= 2:
                    sp.wait_ge(*head_loaded[g - 2].at(b, (a, HG - 1)))
                    alone()
                rows = slice(32 * g, 32 * g + 32)
                if g == 0:
                    sp.wait_ge(*S_of(("q", a))[0].emptied(b, ("q", a)))
                    alone()
                for n, part in enumerate((q_lo, q_hi, q_hi)):
                    sp.dma_start(q_stack[n:P:4, g % 2, :].bitcast(F32),
                                 part[rows, :].bitcast(F32)).then_inc(*q_stack_loaded[g].by_key((a, n)))
                if g == 0:
                    sp.wait_ge(*S_of(("k", a))[0].emptied(b, ("k", a)))
                    alone()
                for n, part in enumerate((k_hi, k_lo, k_hi)):
                    sp.dma_start(k_stack[n:P:4, g, :].bitcast(F32),
                                 part[rows, :].bitcast(F32)).then_inc(*k_stack_loaded[g].by_key((a, n)))
                sp.wait_ge(*q_stack_loaded[g].at(b, (a, 2)))
                alone()
                for j in range(HG):
                    rows = slice(32 * j, 32 * j + (32 if j < HG - 1 else 31))
                    sp.dma_start(q_head[rows, HG * g + j, :].bitcast(F32),
                                 q_stack[rows, g % 2, :].bitcast(F32)).then_inc(*head_loaded[g].by_key((a, j)))

            def negmax_load(b, a, g):
                step = ("negmax", g)
                sp.wait_ge(*bank_m.emptied(b, (a, *step)))
                alone()
                sp.dma_start(q_head[P - 1:P, HG * g:HG * g + HG, :].bitcast(F32),
                             negmax[:, g % 2, :].bitcast(F32)).then_inc(*negmax_loaded.by_key((a, g)))

            with sp.Fori(0, BATCH) as b:
                sp.wait_ge(turn_free, b + 1)
                alone()
                sp.dma_start(x_in[:, :, :], x[b].rearrange("(t p) d -> p t d", p=P)).then_inc(*x_loaded.by_key("x"))
                for a in ATTS:
                    if a == C3:
                        sp.wait_ge(*index_ready.at(b, SEQ))
                        alone()
                        for k in range(2):
                            e = sp.value_load(i8[0:1, 0, k:k + 1], min_val=0, max_val=E - 1)
                            sp.dma_start(w1_raw[:, k, :], w1_seq[e]).then_inc(*seq_w_loaded.by_key(3 * k))
                            sp.dma_start(b1_raw[:, k, :], b1_seq[e]).then_inc(*seq_w_loaded.by_key(3 * k + 1))
                            sp.dma_start(w2_raw[:, k, :, :], w2_seq[e]).then_inc(*seq_w_loaded.by_key(3 * k + 2))
                    for g in range(G + 1):
                        if g < G:
                            stack_loads(b, a, g)
                        if g:
                            negmax_load(b, a, g - 1)
                sp.wait_ge(*y_ready.at(b, "y"))
                alone()
                sp.dma_start(out[b].rearrange("(t p) d -> p t d", p=P), y_out[:, :, :]).then_inc(*stored.by_key("out"))
                sp.wait_ge(*stored.at(b, "out"))
                alone()

        @block.gpsimd
        def _(pool):
            pool.memset(ident[:, :], 0.0).then_inc(pool_setup, 1)
            pool.memset(ident_b[:, :], 0.0).then_inc(pool_setup, 1)
            pool.memset(causal_b[:, :], 0.0).then_inc(pool_setup, 1)
            pool.memset(causal_kq[:, :], 0.0).then_inc(pool_setup, 1)
            pool.wait_ge(pool_setup, 4)
            for m in (ident, ident_b):
                pool.affine_select(out=m[:, :], in_=m[:, :], compare_op=ALU.not_equal, fill=1.0, base=0,
                                   pattern=[[-1, P]], channel_multiplier=1).then_inc(pool_setup, 1)
            pool.affine_select(out=causal_b[:, :], in_=causal_b[:, :], compare_op=ALU.is_ge, fill=NEG, base=0,
                               pattern=[[-1, P]], channel_multiplier=1).then_inc(pool_setup, 1)
            pool.affine_select(out=causal_kq[:, :], in_=causal_kq[:, :], compare_op=ALU.is_ge, fill=NEG, base=0,
                               pattern=[[1, P]], channel_multiplier=-1).then_inc(pool_setup, 1)
            pool.iota(iota8[:, :], [[1, E]], base=0, channel_multiplier=0,
                      allow_small_or_imprecise_dtypes=True).then_inc(pool_setup, 1)
            pool.memset(minus_half[:, :], -0.5).then_inc(pool_setup, 1)
            pool.memset(ones_b[:, :], 1.0).then_inc(pool_setup, 1)
            pool.memset(v_ones[:, :, :, :], 1.0).then_inc(pool_setup, 1)
            pool.memset(q_head[:, :, :].bitcast(F32), 0.0).then_inc(pool_setup, 1)
            pool.memset(q_stack[:, :, :].bitcast(F32), 0.0).then_inc(pool_setup, 1)
            pool.memset(k_stack[:, :, :].bitcast(F32), 1.0).then_inc(pool_setup, 1)

            def rstd_of(b, n):
                pool.wait_ge(*var_ready.at(b, n))
                pool.tensor_tensor(rstd[:, :], var_eps[:, :], minus_half[:, :], ALU.pow).then_inc(*rstd_ready.by_key(n))

            with pool.Fori(0, BATCH) as b:
                pool.wait_ge(turn_free, b + 1)
                rstd_of(b, LN_IN)
                rstd_of(b, LN_A1)
                rstd_of(b, LN_M1)
                rstd_of(b, LN_A2)
                rstd_of(b, LN_M2)
                rstd_of(b, LN_MID)
                for t in range(NT):
                    for e in range(1, E):
                        key = ("glu", t, e // 2)
                        pool.wait_ge(*T_of(key)[0].emptied(b, key))
                        if e > 1:
                            pool.wait_ge(*u_added.at(b, (t, e - 1)))
                        first = glu_u[:, 0, :] if e == 1 else glu_acc[:, t, :]
                        pool.tensor_tensor(glu_acc[:, t, :], first, glu_u[:, e % 4, :],
                                           ALU.add).then_inc(*u_added.by_key((t, e)))
                rstd_of(b, LN_C)

        @block.scalar
        def _(act):
            act.wait_ge(loaded, 16 * 11)
            for n, (hi, e0) in enumerate([(w1_hi, 0), (w1_hi, 4), (wg_hi, 0), (wg_hi, 4)]):
                act.wait_ge(stage_loaded[n % 2], 16 * (n // 2 + 1))
                act.activation(hi[:, e0:e0 + 4, :], stage[:, 4 * (n % 2):4 * (n % 2) + 4, :], ACT.Copy)\
                   .then_inc(stage_hi, 1)

            def attention(b, a):
                for w, hi in (("q", q_hi), ("k", k_hi)):
                    bank, ps = S_of((w, a))
                    act.wait_ge(*bank.filled(b, (w, a)))
                    if a and w == "q":
                        for g in range(G):
                            act.wait_ge(*q_stack_loaded[g].at(b, (a - 1, 2)))
                            act.wait_ge(*k_stack_loaded[g].at(b, (a - 1, 2)))
                    if a in COL_QB:
                        c = COL_QB[a] + (w == "k")
                        done = act.activation(hi[:, :], ps, ACT.Identity, bias=col[:, c:c + 1])
                    else:
                        done = act.activation(hi[:, :], ps, ACT.Copy)
                    done.then_inc(*qk_hi_ready.by_key((a, w)))
                pieces = prob_pieces(a)
                for step in STEPS[a]:
                    if step[0] == "negmax":
                        g = step[1]
                        act.wait_ge(*bank_m.filled(b, (a, *step)))
                        n = NEGMAX.index((a, g))
                        if n >= 2:
                            act.wait_ge(*negmax_loaded.at(b, NEGMAX[n - 2]))
                        act.activation(negmax[:, g % 2, :], ps_m[0:HG * NT, 0:P], ACT.Copy,
                                       scale=-1.0).then_inc(*bank_m.empties((a, *step)))
                    elif step[0] == "prob":
                        g, i = step[1:]
                        kt, heads = pieces[i]
                        w = S - kt * P if CAUSAL[a] else S
                        n = len(heads)
                        slot, ps = T_of((a, *step))
                        act.wait_ge(*slot.filled(b, (a, *step)))
                        if heads[0] == 0:
                            act.wait_ge(*slot_free(b, (a, g, kt)))
                        dst = probs_of((a, g, kt))[:, heads[0] * w:(heads[0] + n) * w]
                        src = ps[:, 0:n * w] if S % w == 0 else ps.rearrange("p (h q) -> p h q", h=n)[:, :, 0:w]
                        if S % w:
                            dst = dst.rearrange("p (h q) -> p h q", h=n)
                        act.activation(dst, src, ACT.Exp, scale=SCALE[a]).then_inc(*slot.empties((a, *step)))
                    elif step[0] == "value" and step[2] == NT - 1:
                        g = step[1]
                        act.wait_ge(*bank_o.filled(b, (a, g)))
                        n = GROUPS.index((a, g))
                        if n >= 2:
                            before = GROUPS[n - 2]
                            act.wait_ge(*bank_m.filled(b, (before[0], "unstack", before[1])))
                        act.activation(o_sb[:, g % 2, :], ps_o[:, :], ACT.Copy).then_inc(*bank_o.empties((a, g)))
                act.wait_ge(*bank_m.filled(b, ("attT", a)))
                act.activation(attT[:, :], ps_m[:, :], ACT.Copy).then_inc(*bank_m.empties(("attT", a)))

            def upper_part(b, ln):
                act.wait_ge(*bank_m.emptied(b, ("ln", ln)))
                act.activation(h_hi[:, :], hT[:, :], ACT.Copy).then_inc(*hi_ready.by_key(ln))

            def gate_exp(b, m):
                act.wait_ge(*gate_in_ready.at(b, m))
                n = 1 if m == SEQ else NT
                act.activation(ex[:, 0:n, :], ex_in[:, 0:n, :], ACT.Exp).then_inc(*gate_exp_ready.by_key(m))

            def gelu_moe(b, m, experts):
                gate_exp(b, m)
                if m == SEQ:
                    act.wait_ge(*seq_w_loaded.at(b, 5))
                    act.activation(ws_hi[:, :, :], w1_raw[:, :, :], ACT.Copy).then_inc(*seq_hi_ready.by_key(SEQ))
                for e in range(experts):
                    for half in range(2):
                        key = ("up", m, e, half)
                        slot, ps = T_of(key)
                        act.wait_ge(*slot.filled(b, key))
                        if half == 0:
                            act.wait_ge(*slot_free(b, (m, e)))
                        for c in (2 * half, 2 * half + 1):
                            bias = col[:, COL_EB1 + NC * e + c:COL_EB1 + NC * e + c + 1] if m == TOKEN \
                                else b1_raw[:, e, c:c + 1]
                            done = act.activation(probs_of((m, e))[:, c * S:(c + 1) * S],
                                                  ps[:, (c % 2) * S:(c % 2 + 1) * S], ACT.Gelu, bias=bias)
                        done.then_inc(*slot.empties(key))
                    if e == 1:
                        act.wait_ge(*bank_m.filled(b, ("cwT", m)))
                        n = P if m == SEQ else S
                        act.activation(cwT[:, 0:n], ps_m[0:E, 0:n], ACT.Copy).then_inc(*bank_m.empties(("cwT", m)))

            def glu_moe(b):
                gate_exp(b, GATED)
                for n, (t, pair) in enumerate(PAIRS):
                    key = ("glu", t, pair)
                    slot, ps = T_of(key)
                    act.wait_ge(*slot.filled(b, key))
                    gates = ps.rearrange("p (k c) -> p k c", k=2)[:, :, GLU:2 * GLU]
                    act.activation(glu_sig[:, n % 2, :, :], gates, ACT.Sigmoid).then_inc(*sig_ready.by_key((t, pair)))
                slot, ps = T_of(("gluT",))
                act.wait_ge(*slot.filled(b, ("gluT",)))
                act.activation(gluT[:, :, :], ps.rearrange("p (k c) -> p k c", k=2),
                               ACT.Copy).then_inc(*slot.empties(("gluT",)))

            with act.Fori(0, BATCH) as b:
                act.wait_ge(turn_free, b + 1)
                attention(b, A0)
                attention(b, B1)
                upper_part(b, LN_M1)
                gelu_moe(b, TOKEN, E)
                attention(b, B2)
                upper_part(b, LN_M2)
                gelu_moe(b, SEQ, 2)
                upper_part(b, LN_MID)
                glu_moe(b)
                attention(b, C3)

        @block.vector
        def _(dve):
            steps = [0]

            def stand_alone():
                dve.sem_inc(dve_passed, 1)

            def chain(b, instruction, alone=False):
                steps[0] += 1
                instruction.then_inc(chained, 1)
                dve.wait_ge(chained, b * CHAIN + steps[0])
                if alone:
                    stand_alone()

            dve.wait_ge(loaded, 16 * 11)
            for n, (hi, lo, e0) in enumerate([(w1_hi, w1_lo, 0), (w1_hi, w1_lo, 4), (wg_hi, wg_lo, 0), (wg_hi, wg_lo, 4)]):
                dve.wait_ge(stage_hi, n + 1)
                dve.tensor_tensor(lo[:, e0:e0 + 4, :], stage[:, 4 * (n % 2):4 * (n % 2) + 4, :],
                                  hi[:, e0:e0 + 4, :].bitcast(F32), ALU.subtract).then_inc(stage_lo, 1)
            dve.wait_ge(b1_loaded, 16)
            for part in range(3):
                dve.tensor_copy(b1_parts[:, part, :], b1_rest[:, part, :]).then_inc(b1_split, 1)
                if part < 2:
                    dve.wait_ge(b1_split, part + 1)
                    dve.tensor_tensor(b1_rest[:, part + 1, :], b1_rest[:, part, :], b1_parts[:, part, :],
                                      ALU.subtract).then_inc(b1_subtracted, 1)
                    dve.wait_ge(b1_subtracted, part + 1)
            dve.wait_ge(b1_placed, 48)
            dve.wait_ge(pool_setup, 15)
            dve.memset(w_sum[:, :], 0.0).then_inc(turn_free, 1)

            def layer_norm(b, n, src, dst):
                for t in range(NT):
                    last = dve.bn_stats(stats[:, t, :], src[:, t, :])
                chain(b, last, alone=True)
                for t in range(NT):
                    last = dve.bn_aggr(mv[:, t, :], stats[:, t, :])
                chain(b, last)
                dve.tensor_scalar(var_eps[:, :], mv[:, :, 1], EPS, None, ALU.add).then_inc(*var_ready.by_key(n))
                dve.wait_ge(*rstd_ready.at(b, n))
                for t in range(NT):
                    last = dve.tensor_scalar(dst[:, t, :], src[:, t, :], mv[:, t, 0:1], rstd[:, t:t + 1],
                                             ALU.subtract, ALU.mult)
                last.then_inc(*z_ready.by_key(n))
                dve.wait_ge(*bank_m.filled(b, ("ln", n)))
                c = COL_LN.get(n)
                if c is None:
                    done = dve.tensor_copy(hT[:, :], ps_m[:, :])
                else:
                    done = dve.tensor_scalar(hT[:, :], ps_m[:, :], col[:, c:c + 1], col[:, c + 1:c + 2],
                                             ALU.mult, ALU.add)
                done.then_inc(*bank_m.empties(("ln", n)))

            def attention(b, a):
                for w, hi, lo in (("q", q_hi, q_lo), ("k", k_hi, k_lo)):
                    bank, ps = S_of((w, a))
                    dve.wait_ge(*qk_hi_ready.at(b, (a, w)))
                    c = COL_QB[a] + (w == "k") if a in COL_QB else None
                    bias = 0.0 if c is None else col[:, c:c + 1]
                    dve.scalar_tensor_tensor(lo[:, :], ps, bias, hi[:, :].bitcast(F32),
                                             ALU.add, ALU.subtract).then_inc(*bank.empties((w, a)))
                dve.wait_ge(*bank_m.filled(b, ("v", a)))
                for t in range(NT):
                    v = ps_m[:, t * D:(t + 1) * D].rearrange("p (h e) -> p h e", h=H)
                    if a in COL_QB:
                        last = dve.tensor_tensor(v_ones[:, t, :, 0:HD], v,
                                                 bv_bc[:, a - B1, :].rearrange("p (h e) -> p h e", h=H), ALU.add)
                    else:
                        last = dve.tensor_copy(v_ones[:, t, :, 0:HD], v)
                last.then_inc(*bank_m.empties(("v", a)))
                pieces = max_pieces(a)
                for step in STEPS[a]:
                    if step[0] == "max":
                        g, i = step[1:]
                        qt, heads = pieces[i]
                        w = (qt + 1) * P if CAUSAL[a] else S
                        n = GROUPS.index((a, g))
                        if i == 0 and n >= 2:
                            before = GROUPS[n - 2]
                            dve.wait_ge(*bank_m.filled(b, (before[0], "negmax", before[1])))
                        bank, ps = S_of((a, *step))
                        dve.wait_ge(*bank.filled(b, (a, *step)))
                        dst = mx[:, g % 2, :].rearrange("p (j t) -> p t j", t=NT)[:, qt, heads[0]:heads[-1] + 1]
                        src = ps[:, 0:len(heads) * w].rearrange("p (h k) -> p h k", k=w)
                        dve.tensor_reduce(dst, src, axis=AX.X, op=ALU.max).then_inc(*bank.empties((a, *step)))
                    elif step[0] == "unstack":
                        g = step[1]
                        dve.wait_ge(*bank_m.filled(b, (a, *step)))
                        o = ps_m[:, :].rearrange("p (t j r) -> p t j r", t=NT, j=HG)
                        chain(b, dve.reciprocal(rden[:, :, :], o[:, :, :, HD]))
                        dst = att[:, :, :].rearrange("p t (h e) -> p t h e", h=H)[:, :, HG * g:HG * g + HG, :]
                        share = rden[:, :, :].rearrange("p t (j o) -> p t j o", o=1).broadcast_to([P, NT, HG, HD])
                        dve.tensor_tensor(dst, o[:, :, :, 0:HD], share, ALU.mult).then_inc(*bank_m.empties((a, *step)))

            def add_attention(b, a, dst, add, bias_row):
                dve.wait_ge(*bank_m.filled(b, ("y", a)))
                y = ps_m[:, :].rearrange("p (t d) -> p t d", t=NT)
                dve.tensor_tensor(dst[:, :, :], y, add[:, :, :], ALU.add).then_inc(*bank_m.empties(("y", a)))
                dve.wait_ge(*bank_m.emptied(b, ("y", a)))
                bias = out_bc[:, bias_row:bias_row + 1, :].broadcast_to([P, NT, D])
                chain(b, dve.tensor_tensor(dst[:, :, :], dst[:, :, :], bias, ALU.add))

            def lower_part(b, ln):
                dve.wait_ge(*hi_ready.at(b, ln))
                dve.tensor_tensor(h_lo[:, :], hT[:, :], h_hi[:, :].bitcast(F32),
                                  ALU.subtract).then_inc(*lo_ready.by_key(ln))

            def gating(b, m):
                n = 1 if m == SEQ else NT
                dve.wait_ge(*bank_m.filled(b, ("logits", m)))
                logits = ps_m[:, 0:n * E].rearrange("p (t e) -> p t e", e=E)
                if m == GATED:
                    done = dve.tensor_copy(lg[:, 0:n, :], logits)
                else:
                    done = dve.tensor_tensor(lg[:, 0:n, :], logits,
                                             gate_bc[:, m:m + 1, :].broadcast_to([P, n, E]), ALU.add)
                done.then_inc(*bank_m.empties(("logits", m)))
                dve.wait_ge(*bank_m.emptied(b, ("logits", m)))
                stand_alone()
                for t in range(n):
                    last = dve.max(v8[:, t, :], lg[:, t, :])
                chain(b, last, alone=True)
                for t in range(n):
                    last = dve.max_index(i8[:, t, :], v8[:, t, :], lg[:, t, :])
                last.then_inc(*index_ready.by_key(m))
                dve.tensor_tensor(ex_in[:, 0:n, 0:E], lg[:, 0:n, :], v8[:, 0:n, 0:1].broadcast_to([P, n, E]),
                                  ALU.subtract)
                dve.tensor_tensor(ex_in[:, 0:n, E:E + 1], v8[:, 0:n, 1:2], v8[:, 0:n, 0:1],
                                  ALU.subtract).then_inc(*gate_in_ready.by_key(m))
                dve.wait_ge(*index_ready.at(b, m))
                dve.tensor_copy(i_f[:, 0:n, :], i8[:, 0:n, 0:2])
                dve.wait_ge(*gate_exp_ready.at(b, m))
                second = ex[:, 0:n, E]
                if m == GATED:
                    chain(b, dve.tensor_reduce(den[:, 0:n], ex[:, 0:n, 0:E], axis=AX.X, op=ALU.add))
                    chain(b, dve.tensor_scalar(den[:, 0:n], den[:, 0:n], 1e-9, 1.0, ALU.mult, ALU.add))
                    chain(b, dve.tensor_tensor(den[:, 0:n], den[:, 0:n], second, ALU.add))
                else:
                    chain(b, dve.tensor_scalar(den[:, 0:n], second, 1.0, None, ALU.add))
                chain(b, dve.reciprocal(w_first[:, 0:n], den[:, 0:n]))
                chain(b, dve.tensor_tensor(w_second[:, 0:n], w_first[:, 0:n], second, ALU.mult))
                for t in range(n):
                    dve.tensor_scalar(cw1[:, t, :], iota8[:, :], i_f[:, t, 0:1], w_first[:, t:t + 1],
                                      ALU.is_equal, ALU.mult)
                    last = dve.tensor_scalar(cw2[:, t, :], iota8[:, :], i_f[:, t, 1:2], w_second[:, t:t + 1],
                                             ALU.is_equal, ALU.mult)
                if m == GATED:
                    last = dve.tensor_tensor(w_sum[:, :], w_first[:, :], w_second[:, :], ALU.add)
                chain(b, last)
                dve.tensor_tensor(cw[:, 0:n, :], cw1[:, 0:n, :], cw2[:, 0:n, :], ALU.add).then_inc(*cw_ready.by_key(m))

            def gelu_moe(b, m, experts):
                gating(b, m)
                if m == SEQ:
                    dve.wait_ge(*seq_hi_ready.at(b, SEQ))
                    dve.tensor_tensor(ws_lo[:, :, :], w1_raw[:, :, :], ws_hi[:, :, :].bitcast(F32),
                                      ALU.subtract).then_inc(*seq_lo_ready.by_key(SEQ))
                dve.wait_ge(*bank_m.filled(b, ("b2", m)))
                y = ps_m[:, :].rearrange("p (t d) -> p t d", t=NT)
                dve.tensor_tensor(res[:, :, :], y, res[:, :, :], ALU.add).then_inc(*bank_m.empties(("b2", m)))
                dve.wait_ge(*bank_m.emptied(b, ("b2", m)))
                dve.wait_ge(*cw_ready.at(b, m))
                for e in range(experts):
                    key = ("down", m, e)
                    bank, ps = S_of(key)
                    dve.wait_ge(*bank.filled(b, key))
                    for t in range(NT):
                        if m == TOKEN:
                            share = cw[:, t, e:e + 1]
                        else:
                            share = (w_first, w_second)[e][:, 0:1]
                        done = dve.scalar_tensor_tensor(res[:, t, :], ps[:, t * D:(t + 1) * D], share, res[:, t, :],
                                                        ALU.mult, ALU.add)
                    done.then_inc(*bank.empties(key))
                    dve.wait_ge(*bank.emptied(b, key))

            def glu_moe(b):
                gating(b, GATED)
                dve.wait_ge(*cw_ready.at(b, GATED))
                for n, (t, pair) in enumerate(PAIRS):
                    key = ("glu", t, pair)
                    slot, ps = T_of(key)
                    dve.wait_ge(*sig_ready.at(b, (t, pair)))
                    if n >= 2:
                        tb, pb = PAIRS[n - 2]
                        dve.wait_ge(*u_added.at(b, (tb, 2 * pb + 1)))
                    for k in range(2):
                        e = 2 * pair + k
                        done = dve.scalar_tensor_tensor(glu_u[:, e % 4, :], ps[:, k * S:k * S + GLU], cw[:, t, e:e + 1],
                                                        glu_sig[:, n % 2, k, :], ALU.mult, ALU.mult)
                    done.then_inc(*slot.empties(key))
                dve.wait_ge(*bank_m.filled(b, ("glu_y",)))
                y = ps_m[:, :].rearrange("p (t d) -> p t d", t=NT)
                dve.tensor_tensor(y_out[:, :, :], y, res[:, :, :], ALU.add).then_inc(*bank_m.empties(("glu_y",)))
                dve.wait_ge(*bank_m.emptied(b, ("glu_y",)))
                chain(b, dve.tensor_tensor(y_out[:, :, :], y_out[:, :, :], xn[:, :, :], ALU.add))
                for t in range(NT):
                    last = dve.scalar_tensor_tensor(y_out[:, t, :], bo_bc[:, :], w_sum[:, t:t + 1], y_out[:, t, :],
                                                    ALU.mult, ALU.add)
                chain(b, last)

            with dve.Fori(0, BATCH) as b:
                dve.wait_ge(turn_free, b + 1)
                dve.wait_ge(*x_loaded.at(b, "x"))
                layer_norm(b, LN_IN, x_in, xn)
                attention(b, A0)
                add_attention(b, A0, att_a, x_in, 0)
                layer_norm(b, LN_A1, xn, z)
                attention(b, B1)
                add_attention(b, B1, res, xn, 1)
                layer_norm(b, LN_M1, res, z)
                lower_part(b, LN_M1)
                gelu_moe(b, TOKEN, E)
                layer_norm(b, LN_A2, res, z)
                attention(b, B2)
                add_attention(b, B2, res, res, 2)
                layer_norm(b, LN_M2, res, z)
                lower_part(b, LN_M2)
                chain(b, dve.tensor_reduce(h_mean[:, :], hT[:, :], axis=AX.X, op=ALU.add))
                chain(b, dve.tensor_scalar(h_mean[:, :], h_mean[:, :], 1.0 / S, None, ALU.mult))
                dve.tensor_scalar(h_mean_bc[:, :], ident[:, :], 0.0, h_mean[:, :],
                                  ALU.mult, ALU.add).then_inc(*h_mean_ready.by_key(SEQ))
                gelu_moe(b, SEQ, 2)
                chain(b, dve.tensor_tensor(res[:, :, :], res[:, :, :], att_a[:, :, :], ALU.add))
                layer_norm(b, LN_MID, res, xn)
                lower_part(b, LN_MID)
                glu_moe(b)
                layer_norm(b, LN_C, xn, z)
                attention(b, C3)
                dve.wait_ge(*bank_m.filled(b, ("y", C3)))
                y = ps_m[:, :].rearrange("p (t d) -> p t d", t=NT)
                dve.tensor_tensor(y_out[:, :, :], y, y_out[:, :, :], ALU.add).then_inc(*bank_m.empties(("y", C3)))
                dve.wait_ge(*bank_m.emptied(b, ("y", C3)))
                dve.memset(w_sum[:, 0:1], 0.0).then_inc(*y_ready.by_key("y"))
                dve.memset(w_sum[:, 1:2], 0.0).then_inc(turn_free, 1)
            assert steps[0] == CHAIN, steps[0]

        @block.tensor
        def _(pe):
            def transposes(b, src):
                for t in range(NT):
                    last = pe.transpose(ps_m[:, t * P:(t + 1) * P], src[:, t, :], ident[:, :])
                return last

            def layer_norm(b, n, z_of):
                key = ("ln", n)
                pe.wait_ge(*bank_m.free(b, key))
                pe.wait_ge(*z_ready.at(b, n))
                transposes(b, z_of).then_inc(*bank_m.fills(key))

            def attention(b, a):
                h = hT[:, :]
                pe.wait_ge(*bank_m.emptied(b, ("ln", LN_OF_ATT[a])))
                for n, w in enumerate("qk"):
                    bank, ps = S_of((w, a))
                    pe.wait_ge(*bank.free(b, (w, a)))
                    pe.matmul(ps, watt[:, a, n, :], h, start=True, stop=True).then_inc(*bank.fills((w, a)))
                pe.wait_ge(*bank_m.free(b, ("v", a)))
                for t in range(NT):
                    last = pe.matmul(ps_m[:, t * D:(t + 1) * D], h[:, t * P:(t + 1) * P], watt[:, a, 2, :],
                                     start=True, stop=True)
                last.then_inc(*bank_m.fills(("v", a)))
                of_max, of_prob = max_pieces(a), prob_pieces(a)
                v_waited = [False]
                for step in STEPS[a]:
                    key = (a, *step)
                    if step[0] == "max":
                        g, i = step[1:]
                        qt, heads = of_max[i]
                        w = (qt + 1) * P if CAUSAL[a] else S
                        bank, ps = S_of(key)
                        pe.wait_ge(*bank.free(b, key))
                        if i == 0:
                            pe.wait_ge(*k_stack_loaded[g].at(b, (a, 2)))
                            pe.wait_ge(*head_loaded[g].at(b, (a, HG - 1)))
                        for n, j in enumerate(heads):
                            last = pe.matmul(ps[:, n * w:(n + 1) * w], q_head[0:P - 1, HG * g + j, qt * P:(qt + 1) * P],
                                             k_stack[0:P - 1, g, 0:w], start=True, stop=not CAUSAL[a])
                            if CAUSAL[a]:
                                last = pe.matmul(ps[:, n * w + qt * P:(n + 1) * w], ident_b[:, :], causal_b[:, :],
                                                 start=False, stop=True)
                        last.then_inc(*bank.fills(key))
                    elif step[0] == "negmax":
                        g = step[1]
                        pe.wait_ge(*bank_m.free(b, key))
                        final = (a, "max", g, len(of_max) - 1)
                        pe.wait_ge(*S_of(final)[0].emptied(b, final))
                        pe.transpose(ps_m[0:HG * NT, 0:P], mx[:, g % 2, :], ident[:, :]).then_inc(*bank_m.fills(key))
                    elif step[0] == "prob":
                        g, i = step[1:]
                        kt, heads = of_prob[i]
                        first = kt * P if CAUSAL[a] else 0
                        w = S - first
                        slot, ps = T_of(key)
                        pe.wait_ge(*slot.free(b, key))
                        if i == 0:
                            pe.wait_ge(*negmax_loaded.at(b, (a, g)))
                        pitch = w if S % w == 0 else S
                        for n, j in enumerate(heads):
                            last = pe.matmul(ps[:, n * pitch:n * pitch + w], k_stack[:, g, kt * P:(kt + 1) * P],
                                             q_head[:, HG * g + j, first:S], start=True, stop=not CAUSAL[a])
                            if CAUSAL[a]:
                                last = pe.matmul(ps[:, n * pitch:n * pitch + P], ident_b[:, :], causal_kq[:, :],
                                                 start=False, stop=True)
                        last.then_inc(*slot.fills(key))
                    elif step[0] == "value":
                        g, kt = step[1:]
                        first = kt * P if CAUSAL[a] else 0
                        w = S - first
                        if not v_waited[0]:
                            pe.wait_ge(*bank_m.emptied(b, ("v", a)))
                            v_waited[0] = True
                        if kt == 0:
                            pe.wait_ge(*bank_o.free(b, (a, g)))
                        piece = (a, "prob", g, max(i for i, (t, _) in enumerate(of_prob) if t == kt))
                        pe.wait_ge(*T_of(piece)[0].emptied(b, piece))
                        for j in range(HG):
                            last = pe.matmul(ps_o[32 * j:32 * j + 32, first:S], v_ones[:, kt, HG * g + j, :],
                                             probs_of((a, g, kt))[:, j * w:(j + 1) * w],
                                             start=(kt == 0), stop=(kt == NT - 1))
                        if kt == NT - 1:
                            last.then_inc(*bank_o.fills((a, g)))
                        else:
                            last.then_inc(*slot_read.by_key((a, g, kt)))
                    elif step[0] == "unstack":
                        g = step[1]
                        pe.wait_ge(*bank_m.free(b, key))
                        pe.wait_ge(*bank_o.emptied(b, (a, g)))
                        for t in range(NT):
                            last = pe.transpose(ps_m[:, t * P:(t + 1) * P], o_sb[:, g % 2, t * P:(t + 1) * P], ident[:, :])
                        last.then_inc(*bank_m.fills(key))
                pe.wait_ge(*bank_m.free(b, ("attT", a)))
                transposes(b, att).then_inc(*bank_m.fills(("attT", a)))
                pe.wait_ge(*bank_m.emptied(b, ("attT", a)))
                for t in range(NT):
                    last = pe.matmul(ps_m[:, t * D:(t + 1) * D], attT[:, t * P:(t + 1) * P], watt[:, a, 3, :],
                                     start=True, stop=True)
                last.then_inc(*bank_m.fills(("y", a)))

            def logits(b, m, lhs_of, n):
                pe.wait_ge(*bank_m.free(b, ("logits", m)))
                for t in range(n):
                    last = pe.matmul(ps_m[:, t * E:(t + 1) * E], lhs_of(t), gw[:, m, :], start=True, stop=True)
                last.then_inc(*bank_m.fills(("logits", m)))

            def gelu_moe(b, m, ln, experts):
                h = hT[:, :]
                if m == TOKEN:
                    pe.wait_ge(*bank_m.emptied(b, ("ln", ln)))
                    logits(b, m, lambda t: h[:, t * P:(t + 1) * P], NT)
                else:
                    pe.wait_ge(*h_mean_ready.at(b, SEQ))
                    logits(b, m, lambda t: h_mean_bc[:, :], 1)
                pe.wait_ge(*lo_ready.at(b, ln))
                if m == SEQ:
                    pe.wait_ge(*seq_lo_ready.at(b, SEQ))
                hi, lo = (w1_hi, w1_lo) if m == TOKEN else (ws_hi, ws_lo)

                def up(e):
                    for half in range(2):
                        key = ("up", m, e, half)
                        slot, ps = T_of(key)
                        pe.wait_ge(*slot.free(b, key))
                        for c in (2 * half, 2 * half + 1):
                            dst = ps[:, (c % 2) * S:(c % 2 + 1) * S]
                            chunk = slice(c * P, (c + 1) * P)
                            pe.matmul(dst, hi[:, e, chunk], h_hi[:, :], start=True, stop=False)
                            pe.matmul(dst, hi[:, e, chunk], h_lo[:, :], start=False, stop=False)
                            last = pe.matmul(dst, lo[:, e, chunk], h_hi[:, :], start=False, stop=True)
                        last.then_inc(*slot.fills(key))

                def down(e):
                    key = ("down", m, e)
                    bank, ps = S_of(key)
                    pe.wait_ge(*bank.free(b, key))
                    pe.wait_ge(*T_of(("up", m, e, 1))[0].emptied(b, ("up", m, e, 1)))
                    for t in range(NT):
                        for c in range(NC):
                            w2 = w2_sb[:, e, c, :] if m == TOKEN else w2_raw[:, e, c, :]
                            last = pe.matmul(ps[:, t * D:(t + 1) * D],
                                             probs_of((m, e))[:, c * S + t * P:c * S + (t + 1) * P], w2,
                                             start=(c == 0), stop=(c == NC - 1))
                    last.then_inc(*bank.fills(key))

                up(0)
                up(1)
                pe.wait_ge(*bank_m.free(b, ("cwT", m)))
                pe.wait_ge(*cw_ready.at(b, m))
                for t in range(1 if m == SEQ else NT):
                    last = pe.transpose(ps_m[0:E, t * P:(t + 1) * P], cw[:, t, :], ident[:, :])
                last.then_inc(*bank_m.fills(("cwT", m)))
                pe.wait_ge(*bank_m.emptied(b, ("cwT", m)))
                for t in range(NT):
                    at = 0 if m == SEQ else t * P
                    last = pe.matmul(ps_m[:, t * D:(t + 1) * D], cwT[:, at:at + P], eb2_sb[:, m, :], start=True, stop=True)
                last.then_inc(*bank_m.fills(("b2", m)))
                for e in range(experts):
                    down(e)
                    if e + 2 < experts:
                        up(e + 2)

            def glu_moe(b):
                h = hT[:, :]
                pe.wait_ge(*bank_m.emptied(b, ("ln", LN_MID)))
                logits(b, GATED, lambda t: h[:, t * P:(t + 1) * P], NT)
                pe.wait_ge(*lo_ready.at(b, LN_MID))
                for t, pair in PAIRS:
                    key = ("glu", t, pair)
                    slot, ps = T_of(key)
                    pe.wait_ge(*slot.free(b, key))
                    tile = slice(t * P, (t + 1) * P)
                    for k in range(2):
                        e = 2 * pair + k
                        dst = ps[:, k * S:(k + 1) * S]
                        pe.matmul(dst, h_hi[:, tile], wg_hi[:, e, :], start=True, stop=False)
                        pe.matmul(dst, h_hi[:, tile], wg_lo[:, e, :], start=False, stop=False)
                        pe.matmul(dst, h_lo[:, tile], wg_hi[:, e, :], start=False, stop=False)
                        last = pe.matmul(dst, ones_b[:, :], b1g3[:, e * S:(e + 1) * S], start=False, stop=True)
                    last.then_inc(*slot.fills(key))
                key = ("gluT",)
                slot, ps = T_of(key)
                pe.wait_ge(*slot.free(b, key))
                pe.wait_ge(*u_added.at(b, (NT - 1, E - 1)))
                for t in range(NT):
                    for c in range(2):
                        last = pe.transpose(ps[:, c * S + t * P:c * S + (t + 1) * P], glu_acc[:, t, c * P:(c + 1) * P],
                                            ident[:, :])
                last.then_inc(*slot.fills(key))
                pe.wait_ge(*bank_m.free(b, ("glu_y",)))
                pe.wait_ge(*slot.emptied(b, key))
                for t in range(NT):
                    for c in range(2):
                        last = pe.matmul(ps_m[:, t * D:(t + 1) * D], gluT[:, c, t * P:(t + 1) * P], wog[:, c, :],
                                         start=(c == 0), stop=(c == 1))
                last.then_inc(*bank_m.fills(("glu_y",)))

            with pe.Fori(0, BATCH) as b:
                pe.wait_ge(turn_free, b + 1)
                layer_norm(b, LN_IN, xn)
                attention(b, A0)
                layer_norm(b, LN_A1, z)
                attention(b, B1)
                layer_norm(b, LN_M1, z)
                gelu_moe(b, TOKEN, LN_M1, E)
                layer_norm(b, LN_A2, z)
                attention(b, B2)
                layer_norm(b, LN_M2, z)
                gelu_moe(b, SEQ, LN_M2, 2)
                layer_norm(b, LN_MID, xn)
                glu_moe(b)
                layer_norm(b, LN_C, z)
                attention(b, C3)


def kernel(**inputs):
    import numpy as np
    import concourse.bacc as bacc
    from concourse.bass_utils import run_bass_kernel_spmd

    v = {k: np.asarray(a) for k, a in inputs.items()}
    f = np.float32

    def by_head(w):
        full = np.zeros((D, D), f)
        for h in range(H):
            full[h * HD:(h + 1) * HD, h * HD:(h + 1) * HD] = w.T
        return full

    def joined(w):
        return w.transpose(1, 0, 2).reshape(D, D)

    w_att = np.stack([
        np.stack([by_head(v["L0_attn_Wq"]), by_head(v["L0_attn_Wk"]), by_head(v["L0_attn_Wv"]), v["L0_attn_W_out"].T]),
        *(np.stack([v["L0_ffn_wq"][l], v["L0_ffn_wk"][l], v["L0_ffn_wv"][l], v["L0_ffn_wo"][l]]) for l in range(2)),
        np.stack([joined(v["L1_attn_wq"]), joined(v["L1_attn_wk"]), joined(v["L1_attn_wv"]), v["L1_attn_wo"]]),
    ]).transpose(2, 0, 1, 3)
    e_b1 = v["L0_ffn_e_b1"].reshape(2, E, NC, P)
    cols = np.stack([
        v["L0_ffn_ln1_w"][0], v["L0_ffn_ln1_b"][0], v["L0_ffn_ln2_w"][0], v["L0_ffn_ln2_b"][0],
        v["L0_ffn_ln1_w"][1], v["L0_ffn_ln1_b"][1], v["L0_ffn_ln2_w"][1], v["L0_ffn_ln2_b"][1],
        v["L1_attn_ln_w"], v["L1_attn_ln_b"],
        v["L0_ffn_bq"][0], v["L0_ffn_bk"][0], v["L0_ffn_bq"][1], v["L0_ffn_bk"][1],
        *e_b1[0].reshape(E * NC, P),
    ], axis=1)
    e_w2 = v["L0_ffn_e_w2"].reshape(2, E, NC, P, D)
    arrays = {
        "x": v["L0_attn_x"],
        "w_att": w_att,
        "cols": cols,
        "bv_rows": v["L0_ffn_bv"],
        "out_rows": np.stack([v["L0_attn_b_out"], v["L0_ffn_bo"][0], v["L0_ffn_bo"][1]]),
        "gate_w": np.stack([v["L0_ffn_gate_w"][0], v["L0_ffn_gate_w"][1], v["L1_ffn_Wg"].T]).transpose(1, 0, 2),
        "gate_rows": v["L0_ffn_gate_b"],
        "w1_token": v["L0_ffn_e_w1"][0].transpose(1, 0, 2),
        "w2_token": e_w2[0].transpose(2, 0, 1, 3),
        "eb2": v["L0_ffn_e_b2"].transpose(1, 0, 2),
        "w1_seq": v["L0_ffn_e_w1"][1],
        "b1_seq": e_b1[1].transpose(0, 2, 1),
        "w2_seq": e_w2[1].transpose(0, 2, 1, 3),
        "w1_glu": v["L1_ffn_W1"].transpose(2, 0, 1),
        "b1_glu": v["L1_ffn_b1"].reshape(P, E * 2 * GLU // P),
        "wo_glu": v["L1_ffn_Wo"].T.reshape(2, P, D).transpose(1, 0, 2),
        "bo_glu": v["L1_ffn_bo"],
    }
    nc = bacc.Bacc("TRN2", target_bir_lowering=False, num_devices=1)
    arrays = {k: np.ascontiguousarray(a) for k, a in arrays.items()}
    args = {k: nc.dram_tensor(k, a.shape, mybir.dt.from_np(a.dtype), kind="ExternalInput").ap()
            for k, a in arrays.items()}
    out = nc.dram_tensor("out", (BATCH, S, D), F32, kind="ExternalOutput").ap()
    build(nc, *args.values(), out)
    result = run_bass_kernel_spmd(nc, [arrays], core_ids=[0])
    return result.results[0]["out"]
```
